# Optimizing a Trainium2 kernel written in Bass

```python
import numpy as np
import jax
import jax.numpy as jnp

def _softmax(x, axis=-1):
    return jax.nn.softmax(x, axis=axis)

def _gelu(x):
    return jax.nn.gelu(x, approximate=True)

def _silu(x):
    return jax.nn.silu(x)

def _sigmoid(x):
    return jax.nn.sigmoid(x)

def _layernorm(x, axis=-1, eps=1e-05):
    m = jnp.mean(x, axis=axis, keepdims=True)
    v = jnp.var(x, axis=axis, keepdims=True)
    return (x - m) / jnp.sqrt(v + eps)

def _scatter_add(tgt, idx, src, axis=0):
    return tgt.at[idx].add(src)

def _segment_sum(src, seg, n):
    return jax.ops.segment_sum(src, seg, n)
kernel_name = 'mk_dlrm_tower_d1_rec_r8_17b2c2'

def setup_inputs(seed: int=0):
    np.random.seed(seed)
    _w = jnp.asarray

    def _rec_inputs():
        import jax
        import jax.numpy as jnp
        _tk = jax.random.key(seed)
        dense_ctx = jax.random.normal(jax.random.fold_in(_tk, 190), (2048, 16), jnp.float32)
        ids = jnp.stack([jax.random.randint(jax.random.fold_in(_tk, 200 + f), (2048,), 0, v, jnp.int32) for f, v in enumerate([1000, 125000, 12500, 1250, 12500, 125000, 1000, 12500, 125000, 1000, 1000, 1250, 12500, 12500, 1250, 1000, 1250, 12500, 1250, 12500, 1000, 1000, 1000, 12500, 1250, 1250, 1250, 1000, 1250, 1000, 1000, 1000])], axis=1)
        tbl_0 = 0.05 * jax.random.normal(jax.random.fold_in(_tk, 500 + 0), (1000, 64), jnp.float32)
        tbl_1 = 0.05 * jax.random.normal(jax.random.fold_in(_tk, 500 + 1), (125000, 64), jnp.float32)
        tbl_2 = 0.05 * jax.random.normal(jax.random.fold_in(_tk, 500 + 2), (12500, 64), jnp.float32)
        tbl_3 = 0.05 * jax.random.normal(jax.random.fold_in(_tk, 500 + 3), (1250, 64), jnp.float32)
        tbl_4 = 0.05 * jax.random.normal(jax.random.fold_in(_tk, 500 + 4), (12500, 64), jnp.float32)
        tbl_5 = 0.05 * jax.random.normal(jax.random.fold_in(_tk, 500 + 5), (125000, 64), jnp.float32)
        tbl_6 = 0.05 * jax.random.normal(jax.random.fold_in(_tk, 500 + 6), (1000, 64), jnp.float32)
        tbl_7 = 0.05 * jax.random.normal(jax.random.fold_in(_tk, 500 + 7), (12500, 64), jnp.float32)
        tbl_8 = 0.05 * jax.random.normal(jax.random.fold_in(_tk, 500 + 8), (125000, 64), jnp.float32)
        tbl_9 = 0.05 * jax.random.normal(jax.random.fold_in(_tk, 500 + 9), (1000, 64), jnp.float32)
        tbl_10 = 0.05 * jax.random.normal(jax.random.fold_in(_tk, 500 + 10), (1000, 64), jnp.float32)
        tbl_11 = 0.05 * jax.random.normal(jax.random.fold_in(_tk, 500 + 11), (1250, 64), jnp.float32)
        tbl_12 = 0.05 * jax.random.normal(jax.random.fold_in(_tk, 500 + 12), (12500, 64), jnp.float32)
        tbl_13 = 0.05 * jax.random.normal(jax.random.fold_in(_tk, 500 + 13), (12500, 64), jnp.float32)
        tbl_14 = 0.05 * jax.random.normal(jax.random.fold_in(_tk, 500 + 14), (1250, 64), jnp.float32)
        tbl_15 = 0.05 * jax.random.normal(jax.random.fold_in(_tk, 500 + 15), (1000, 64), jnp.float32)
        tbl_16 = 0.05 * jax.random.normal(jax.random.fold_in(_tk, 500 + 16), (1250, 64), jnp.float32)
        tbl_17 = 0.05 * jax.random.normal(jax.random.fold_in(_tk, 500 + 17), (12500, 64), jnp.float32)
        tbl_18 = 0.05 * jax.random.normal(jax.random.fold_in(_tk, 500 + 18), (1250, 64), jnp.float32)
        tbl_19 = 0.05 * jax.random.normal(jax.random.fold_in(_tk, 500 + 19), (12500, 64), jnp.float32)
        tbl_20 = 0.05 * jax.random.normal(jax.random.fold_in(_tk, 500 + 20), (1000, 64), jnp.float32)
        tbl_21 = 0.05 * jax.random.normal(jax.random.fold_in(_tk, 500 + 21), (1000, 64), jnp.float32)
        tbl_22 = 0.05 * jax.random.normal(jax.random.fold_in(_tk, 500 + 22), (1000, 64), jnp.float32)
        tbl_23 = 0.05 * jax.random.normal(jax.random.fold_in(_tk, 500 + 23), (12500, 64), jnp.float32)
        tbl_24 = 0.05 * jax.random.normal(jax.random.fold_in(_tk, 500 + 24), (1250, 64), jnp.float32)
        tbl_25 = 0.05 * jax.random.normal(jax.random.fold_in(_tk, 500 + 25), (1250, 64), jnp.float32)
        tbl_26 = 0.05 * jax.random.normal(jax.random.fold_in(_tk, 500 + 26), (1250, 64), jnp.float32)
        tbl_27 = 0.05 * jax.random.normal(jax.random.fold_in(_tk, 500 + 27), (1000, 64), jnp.float32)
        tbl_28 = 0.05 * jax.random.normal(jax.random.fold_in(_tk, 500 + 28), (1250, 64), jnp.float32)
        tbl_29 = 0.05 * jax.random.normal(jax.random.fold_in(_tk, 500 + 29), (1000, 64), jnp.float32)
        tbl_30 = 0.05 * jax.random.normal(jax.random.fold_in(_tk, 500 + 30), (1000, 64), jnp.float32)
        tbl_31 = 0.05 * jax.random.normal(jax.random.fold_in(_tk, 500 + 31), (1000, 64), jnp.float32)
        _rk = jax.random.fold_in(_tk, 7)
        W_top1 = 0.0441942 * jax.random.normal(jax.random.fold_in(_tk, 801), (512, 512), jnp.float32)
        W_top2 = 0.0441942 * jax.random.normal(jax.random.fold_in(_tk, 802), (512, 256), jnp.float32)
        W_top3 = 0.0625 * jax.random.normal(jax.random.fold_in(_tk, 803), (256, 1), jnp.float32)
        b_top1 = jnp.zeros((512,), jnp.float32)
        b_top2 = jnp.zeros((256,), jnp.float32)
        return (dense_ctx, ids, tbl_0, tbl_1, tbl_2, tbl_3, tbl_4, tbl_5, tbl_6, tbl_7, tbl_8, tbl_9, tbl_10, tbl_11, tbl_12, tbl_13, tbl_14, tbl_15, tbl_16, tbl_17, tbl_18, tbl_19, tbl_20, tbl_21, tbl_22, tbl_23, tbl_24, tbl_25, tbl_26, tbl_27, tbl_28, tbl_29, tbl_30, tbl_31, W_top1, b_top1, W_top2, b_top2, W_top3)
    dense_ctx, ids, tbl_0, tbl_1, tbl_2, tbl_3, tbl_4, tbl_5, tbl_6, tbl_7, tbl_8, tbl_9, tbl_10, tbl_11, tbl_12, tbl_13, tbl_14, tbl_15, tbl_16, tbl_17, tbl_18, tbl_19, tbl_20, tbl_21, tbl_22, tbl_23, tbl_24, tbl_25, tbl_26, tbl_27, tbl_28, tbl_29, tbl_30, tbl_31, W_top1, b_top1, W_top2, b_top2, W_top3 = _rec_inputs()

    def _L0_rec_setup():
        import jax, jax.numpy as jnp
        import numpy as np
        B = 256
        NUM_FIELDS = 32
        EMBED = 64
        P = NUM_FIELDS * (NUM_FIELDS - 1) // 2
        _ROW, _COL = np.triu_indices(NUM_FIELDS, k=1)
        ROW_IDX = jnp.asarray(_ROW, dtype=jnp.int32)
        COL_IDX = jnp.asarray(_COL, dtype=jnp.int32)
        key = jax.random.key(seed)
        k1, k2 = jax.random.split(key)
        emb_inputs = jax.random.normal(k1, (B, NUM_FIELDS, EMBED), dtype=jnp.float32)
        fan_in = P * EMBED
        fan_out = EMBED
        std = float(np.sqrt(2.0 / (fan_in + fan_out)))
        kernel = jax.random.normal(k2, (EMBED, P, EMBED), dtype=jnp.float32) * std
        return {'emb_inputs': emb_inputs, 'kernel': kernel}
    _L0_rec_all = _L0_rec_setup()
    _L0_rec_in = {k: v for k, v in _L0_rec_all.items() if k in ('kernel',)}
    del _L0_rec_all
    return {'dense_ctx': dense_ctx, 'ids': ids, 'tbl_0': tbl_0, 'tbl_1': tbl_1, 'tbl_2': tbl_2, 'tbl_3': tbl_3, 'tbl_4': tbl_4, 'tbl_5': tbl_5, 'tbl_6': tbl_6, 'tbl_7': tbl_7, 'tbl_8': tbl_8, 'tbl_9': tbl_9, 'tbl_10': tbl_10, 'tbl_11': tbl_11, 'tbl_12': tbl_12, 'tbl_13': tbl_13, 'tbl_14': tbl_14, 'tbl_15': tbl_15, 'tbl_16': tbl_16, 'tbl_17': tbl_17, 'tbl_18': tbl_18, 'tbl_19': tbl_19, 'tbl_20': tbl_20, 'tbl_21': tbl_21, 'tbl_22': tbl_22, 'tbl_23': tbl_23, 'tbl_24': tbl_24, 'tbl_25': tbl_25, 'tbl_26': tbl_26, 'tbl_27': tbl_27, 'tbl_28': tbl_28, 'tbl_29': tbl_29, 'tbl_30': tbl_30, 'tbl_31': tbl_31, 'W_top1': W_top1, 'b_top1': b_top1, 'W_top2': W_top2, 'b_top2': b_top2, 'W_top3': W_top3, 'L0_rec_kernel': _L0_rec_in['kernel']}

def reference(dense_ctx, ids, tbl_0, tbl_1, tbl_2, tbl_3, tbl_4, tbl_5, tbl_6, tbl_7, tbl_8, tbl_9, tbl_10, tbl_11, tbl_12, tbl_13, tbl_14, tbl_15, tbl_16, tbl_17, tbl_18, tbl_19, tbl_20, tbl_21, tbl_22, tbl_23, tbl_24, tbl_25, tbl_26, tbl_27, tbl_28, tbl_29, tbl_30, tbl_31, W_top1, b_top1, W_top2, b_top2, W_top3, L0_rec_kernel):
    import jax
    import jax.numpy as jnp

    def _L0_rec_ref(emb_inputs, kernel):
        import jax, jax.numpy as jnp
        import numpy as np
        B = 256
        NUM_FIELDS = 32
        EMBED = 64
        P = NUM_FIELDS * (NUM_FIELDS - 1) // 2
        _ROW, _COL = np.triu_indices(NUM_FIELDS, k=1)
        ROW_IDX = jnp.asarray(_ROW, dtype=jnp.int32)
        COL_IDX = jnp.asarray(_COL, dtype=jnp.int32)
        p = emb_inputs[:, ROW_IDX]
        q = emb_inputs[:, COL_IDX]
        return jnp.einsum('bne,hne,bnh->bn', p, kernel, q)
    e = jnp.stack([tbl_0[ids[:, 0]], tbl_1[ids[:, 1]], tbl_2[ids[:, 2]], tbl_3[ids[:, 3]], tbl_4[ids[:, 4]], tbl_5[ids[:, 5]], tbl_6[ids[:, 6]], tbl_7[ids[:, 7]], tbl_8[ids[:, 8]], tbl_9[ids[:, 9]], tbl_10[ids[:, 10]], tbl_11[ids[:, 11]], tbl_12[ids[:, 12]], tbl_13[ids[:, 13]], tbl_14[ids[:, 14]], tbl_15[ids[:, 15]], tbl_16[ids[:, 16]], tbl_17[ids[:, 17]], tbl_18[ids[:, 18]], tbl_19[ids[:, 19]], tbl_20[ids[:, 20]], tbl_21[ids[:, 21]], tbl_22[ids[:, 22]], tbl_23[ids[:, 23]], tbl_24[ids[:, 24]], tbl_25[ids[:, 25]], tbl_26[ids[:, 26]], tbl_27[ids[:, 27]], tbl_28[ids[:, 28]], tbl_29[ids[:, 29]], tbl_30[ids[:, 30]], tbl_31[ids[:, 31]]], axis=1)
    z = _L0_rec_ref(e, L0_rec_kernel)
    z = z.reshape(z.shape[0], -1)
    h = jnp.concatenate([z, dense_ctx], axis=1)
    h = jnp.maximum(h @ W_top1 + b_top1, 0.0)
    h = jnp.maximum(h @ W_top2 + b_top2, 0.0)
    y = h @ W_top3
    return y

_drawn_inputs = setup_inputs


def setup_inputs(seed=0):
    import zlib

    import numpy as np

    out = dict(_drawn_inputs(seed))
    spreads = {'b_top1': (0.0, 0.1), 'b_top2': (0.0, 0.1)}
    factors = {'tbl_0': 8.0,
     'tbl_1': 8.0,
     'tbl_2': 8.0,
     'tbl_3': 8.0,
     'tbl_4': 8.0,
     'tbl_5': 8.0,
     'tbl_6': 8.0,
     'tbl_7': 8.0,
     'tbl_8': 8.0,
     'tbl_9': 8.0,
     'tbl_10': 8.0,
     'tbl_11': 8.0,
     'tbl_12': 8.0,
     'tbl_13': 8.0,
     'tbl_14': 8.0,
     'tbl_15': 8.0,
     'tbl_16': 8.0,
     'tbl_17': 8.0,
     'tbl_18': 8.0,
     'tbl_19': 8.0,
     'tbl_20': 8.0,
     'tbl_21': 8.0,
     'tbl_22': 8.0,
     'tbl_23': 8.0,
     'tbl_24': 8.0,
     'tbl_25': 8.0,
     'tbl_26': 8.0,
     'tbl_27': 8.0,
     'tbl_28': 8.0,
     'tbl_29': 8.0,
     'tbl_30': 8.0,
     'tbl_31': 8.0,
     'L0_rec_kernel': 8.0}
    for name, (base, spread) in spreads.items():
        noise = np.random.default_rng([zlib.crc32(name.encode()), seed]).standard_normal(out[name].shape)
        drawn = base * np.exp(spread * noise) if base else spread * noise
        out[name] = jnp.asarray(drawn.astype(out[name].dtype))
    for name, factor in factors.items():
        out[name] = (out[name] * factor).astype(out[name].dtype)
    return out
```

```python
from contextlib import ExitStack

import concourse.bass as bass
from concourse import mybir

ALU = mybir.AluOpType
ACT = mybir.ActivationFunctionType
AX_X = mybir.AxisListType.X
F32 = mybir.dt.float32
F32R = mybir.dt.float32r
I32 = mybir.dt.int32
U32 = mybir.dt.uint32

P = 128
BANK = 512
QF = 4
SLOT = 16
PRING = 4
ACT_PAIRS = 6


def first_pair(i, fields):
    return i * (fields - 1) - i * (i - 1) // 2


def plan(fields):
    pairs = fields * (fields - 1) // 2
    half = SLOT // 2
    sizes = [SLOT] * (pairs // SLOT - 1) + [half, half]
    assert sum(sizes) == pairs and len(sizes) % PRING == 0
    slots, n = [], 0
    for size in sizes:
        segs, m = [], n
        while m < n + size:
            i = max(r for r in range(fields - 1) if first_pair(r, fields) <= m)
            w = min(first_pair(i + 1, fields), n + size) - m
            segs.append((i, i + 1 + m - first_pair(i, fields), m, w))
            m += w
        slots.append((n, size, segs))
        n += size
    return slots


def dlrm_tower(nc, dense, ids, tables, W1, b1, W2, b2, W3, KT, out):
    B, DC = dense.shape
    NF = len(tables)
    D = tables[0].shape[1]
    H1, H2 = W2.shape
    TILES = B // P
    BODIES = TILES // 2
    NP = NF * (NF - 1) // 2
    QUADS = NF // QF
    KC = W1.shape[0] // P
    M1, M2 = H1 // P, H2 // P
    PB = 2 * P
    HB = BANK // D
    SLOTS = plan(NF)
    NS = len(SLOTS)
    assert NP + DC == KC * P and M1 == KC and D == P // 2 and TILES % 2 == 0

    first_use = [min(s for s, (_, _, g) in enumerate(SLOTS) if any(x[0] // QF == q for x in g)) for q in range(QUADS)]
    last_use = [max(s for s, (_, _, g) in enumerate(SLOTS) if any(x[0] // QF == q for x in g)) for q in range(QUADS)]
    ERING = 4
    TR_AT = {1: (0, 2), 3: (0, 3), 8: (0, 4), 14: (0, 5), 20: (0, 6), 24: (0, 7), 27: (1, 0), 30: (1, 1)}
    CAST_AT = {4: (0, 4), 10: (0, 5), 16: (0, 6), 20: (0, 7), 23: (1, 0), 26: (1, 1), 29: (1, 2), 31: (1, 3)}
    for s, (ahead, q) in TR_AT.items():
        before = q + QUADS * ahead - ERING
        assert before < 0 or s >= last_use[before]
        assert s < first_use[q] + NS * ahead
    Z_AT = 4
    L1_AT = {8 + n: (n // 2, n % 2) for n in range(2 * M1)}
    L2_AT = {18 + n: (n // 2, n % 2) for n in range(2 * M2)}
    L3_AT = 25
    EVAC_AT = {6: 0, 13: 1, 17: 2, 23: 3, 27: 4}
    BATCHES = 6

    ctx = ExitStack()
    with ctx:
        def sb(name, shape, dt):
            return ctx.enter_context(nc.sbuf_tensor(name, shape, dt))

        def sem(name):
            return ctx.enter_context(nc.semaphore(name))

        kst = sb("kst", [P, NP * D], F32R)
        E = sb("E", [P, 2, NF, D], F32)
        nat = sb("nat", [P, 2, QF, 2, D], F32R)
        eA = sb("eA", [P, ERING, QF, P], F32R)
        eB = sb("eB", [P, ERING, QF, P], F32R)
        prod = sb("prod", [P, PRING, SLOT * D], F32)
        z = sb("z", [P, 2, KC * P], F32)
        acts = sb("acts", [P, (KC + M1 + M2) * PB], F32)
        zT = acts[:, 0:KC * PB].rearrange("p (k b) -> p k b", k=KC)
        h1T = acts[:, KC * PB:(KC + M1) * PB].rearrange("p (k b) -> p k b", k=M1)
        h2T = acts[:, (KC + M1) * PB:].rearrange("p (k b) -> p k b", k=M2)
        raw = acts[0:D, 0:2 * SLOT * D].rearrange("p (r c) -> p r c", r=2)
        w1 = sb("w1", [P, KC, H1], F32)
        w2 = sb("w2", [P, M1, H2], F32)
        w3 = sb("w3", [P, M2], F32)
        b1c = sb("b1c", [P, M1], F32)
        b2c = sb("b2c", [P, M2], F32)
        ident = sb("ident", [P, P], F32)
        identr = sb("identr", [P, P], F32R)
        idx = sb("idx", [P, 2, NF], I32)
        y = sb("y", [1, PB], F32)

        T = ctx.enter_context(nc.psum_tensor("T", [P, 2, SLOT * D], F32))
        psE = ctx.enter_context(nc.psum_tensor("psE", [P, BANK], F32))
        psM = ctx.enter_context(nc.psum_tensor("psM", [P, 2, BANK], F32))

        idx_in = [sem(f"idx_in{u}") for u in range(2)]
        gathered = [[sem(f"gathered{u}_{q}") for q in range(QUADS)] for u in range(2)]
        dense_in = [sem(f"dense_in{u}") for u in range(2)]
        weights_in = sem("weights_in")
        k_in = [sem(f"k_in{r}") for r in range(2)]
        kh_done = sem("kh_done")
        k_done = sem("k_done")
        ident_0 = sem("ident_0")
        ident_1 = sem("ident_1")
        identr_done = sem("identr_done")
        cast_done = sem("cast_done")
        low_done = sem("low_done")
        e_transposed = sem("e_transposed")
        a_done = sem("a_done")
        b_done = [sem(f"b_done{r}") for r in range(ERING)]
        t_ready = sem("t_ready")
        mult_done = sem("mult_done")
        dve_reduced = sem("dve_reduced")
        act_reduced = sem("act_reduced")
        mlp_pe = sem("mlp_pe")
        mlp_act = sem("mlp_act")
        y_out = sem("y_out")

        def share(size):
            return size - ACT_PAIRS * size // SLOT

        def bodies(eng, body):
            body(0, True, False)
            with eng.Fori(1, BODIES - 1) as b:
                body(b, False, False)
            body(BODIES - 1, False, True)

        def ordinal(b, batch):
            return (b - 1) * BATCHES + 1 + batch

        def z_read(b, u):
            return ordinal(b, 5) + 1 if u == 0 else ordinal(b + 1, 0) + 1

        block = ctx.enter_context(nc.Block())

        @block.sync
        def _(sp):
            def load_k(c):
                n, size, _ = SLOTS[c]
                if c >= 2:
                    sp.wait_ge(k_done, c - 1)
                sp.dma_start(raw[:, c % 2, 0:size * D], KT[:, n * D:(n + size) * D]).then_inc(k_in[c % 2], 16)

            def load_idx(t, u):
                sp.dma_start(idx[:, u, :], ids[bass.ts(t, P), :]).then_inc(idx_in[u], 16)

            def load_dense(t, u):
                sp.dma_start(z[:, u, NP:NP + DC], dense[bass.ts(t, P), :]).then_inc(dense_in[u], 16)

            def swap_halves(Q, r):
                sp.wait_ge(a_done, Q + 1)
                sp.dma_start(eB[0:D, r].bitcast(F32), eA[D:P, r].bitcast(F32)).then_inc(b_done[r], 16)
                sp.dma_start(eB[D:P, r].bitcast(F32), eA[0:D, r].bitcast(F32)).then_inc(b_done[r], 16)

            def store_y(b):
                sp.wait_ge(mlp_act, ordinal(b, 4) + 1)
                sp.dma_start(out[:, bass.ts(b - 1, PB)], y[:, :]).then_inc(y_out, 16)

            load_idx(0, 0)
            load_k(0)
            load_k(1)
            load_idx(1, 1)
            load_dense(0, 0)
            load_dense(1, 1)
            swap_halves(0, 0)
            swap_halves(1, 1)

            def body(b, first, last):
                for u in range(2):
                    t = 2 * b + u
                    for s in range(NS):
                        if first and u == 0 and s + 2 < NS:
                            load_k(s + 2)
                            if s == 2:
                                sp.dma_start(w1[:, :, :], W1.rearrange("(k p) m -> p k m", p=P)).then_inc(weights_in, 16)
                                sp.dma_start(w2[:, :, :], W2.rearrange("(k p) m -> p k m", p=P)).then_inc(weights_in, 16)
                                sp.dma_start(w3[:, :], W3).then_inc(weights_in, 16)
                                sp.dma_start(b1c[:, :], b1).then_inc(weights_in, 16)
                                sp.dma_start(b2c[:, :], b2).then_inc(weights_in, 16)
                        if s == 10 and not (first and u == 0) and not (last and u == 1):
                            sp.wait_ge(mlp_pe, z_read(b - 1 + u, 1 - u))
                            load_dense(t + 1, 1 - u)
                        if s == 26 and not last:
                            sp.wait_ge(mult_done, NS * t + 1)
                            load_idx(t + 2, u)
                        if s in TR_AT:
                            ahead, q = TR_AT[s]
                            if not (last and u == 1 and ahead):
                                swap_halves(QUADS * (t + ahead) + q, q % ERING)
                        if u == 0 and s == 29 and not first:
                            store_y(b)

            bodies(sp, body)
            store_y(BODIES)
            sp.wait_ge(y_out, 16 * BODIES)

        @block.gpsimd
        def _(pool):
            def gather(b, u, q):
                for f in range(QF * q, QF * q + QF):
                    nc.gpsimd.indirect_dma_start(
                        out=E[:, u, f, :], out_offset=None, in_=tables[f],
                        in_offset=bass.IndirectOffsetOnAxis(ap=idx[:, u, f:f + 1].bitcast(U32), axis=0),
                    ).then_inc(gathered[u][q], 16)

            def low(Q, u, q):
                pool.wait_ge(cast_done, Q + 1)
                nc.gpsimd.tensor_tensor(nat[:, q % 2, :, 1, :], E[:, u, QF * q:QF * q + QF, :],
                                        nat[:, q % 2, :, 0, :].bitcast(F32), ALU.subtract).then_inc(low_done, 1)

            nc.gpsimd.memset(ident[:, :], 0.0).then_inc(ident_0, 1)
            pool.wait_ge(idx_in[0], 16)
            gather(0, 0, 0)
            pool.wait_ge(ident_0, 1)
            nc.gpsimd.affine_select(out=ident[:, :], in_=ident[:, :], compare_op=ALU.not_equal, fill=1.0,
                                    base=0, pattern=[[-1, P]], channel_multiplier=1).then_inc(ident_1, 1)
            gather(0, 0, 1)
            low(0, 0, 0)
            for q in range(2, QUADS):
                gather(0, 0, q)
                if q == 2:
                    low(1, 0, 1)

            def body(b, first, last):
                for u in range(2):
                    t = 2 * b + u
                    more = not (last and u == 1)

                    def ahead(q):
                        if more:
                            gather(b, 1 - u, q)
                    low(QUADS * t + 2, u, 2)
                    if more:
                        pool.wait_ge(idx_in[1 - u], 16 * (b + 1 + u))
                        if not (first and u == 0):
                            pool.wait_ge(mult_done, NS * t)
                    low(QUADS * t + 3, u, 3)
                    for q in range(4, QUADS):
                        ahead(2 * (q - 4))
                        ahead(2 * (q - 4) + 1)
                        low(QUADS * t + q, u, q)
                    if more:
                        low(QUADS * (t + 1), 1 - u, 0)
                        low(QUADS * (t + 1) + 1, 1 - u, 1)

            bodies(pool, body)

        @block.scalar
        def _(act):
            def cast_k(c):
                n, size, _ = SLOTS[c]
                act.wait_ge(k_in[c % 2], 16 * (c // 2 + 1))
                nc.scalar.activation(kst[0:D, n * D:(n + size) * D], raw[:, c % 2, 0:size * D],
                                     ACT.Copy).then_inc(kh_done, 1)

            def cast(Q, b, u, q, start=False):
                act.wait_ge(gathered[u][q], 16 * QF * (b + 1))
                if not start:
                    act.wait_ge(e_transposed, Q - 1)
                nc.scalar.activation(nat[:, q % 2, :, 0, :], E[:, u, QF * q:QF * q + QF, :],
                                     ACT.Copy).then_inc(cast_done, 1)

            def evacuate_quad(Q, q):
                act.wait_ge(e_transposed, Q + 1)
                fields = min(QF, NF - 1 - QF * q)
                nc.scalar.activation(eA[:, q % ERING, 0:fields, :],
                                     psE[:, 0:fields * P].rearrange("p (f b) -> p f b", b=P),
                                     ACT.Copy).then_inc(a_done, 1)

            def mlp_evacuate(b, batch):
                act.wait_ge(mlp_pe, ordinal(b, batch) + 1)
                bank = psM[:, 1 if batch in (1, 3) else 0, :]
                halves = bank.rearrange("p (m b) -> p m b", m=2)
                if batch in (0, 5):
                    u = 1 if batch == 0 else 0
                    last = nc.scalar.activation(zT[:, :, u * P:(u + 1) * P],
                                                bank.rearrange("p (k b) -> p k b", k=KC), ACT.Copy)
                elif batch in (1, 2):
                    for m in range(2):
                        mm = 2 * (batch - 1) + m
                        last = nc.scalar.activation(h1T[:, mm, :], halves[:, m, :], ACT.Relu, bias=b1c[:, mm:mm + 1])
                elif batch == 3:
                    for m in range(M2):
                        last = nc.scalar.activation(h2T[:, m, :], halves[:, m, :], ACT.Relu, bias=b2c[:, m:m + 1])
                else:
                    last = nc.scalar.activation(y[:, :], bank[0:1, 0:PB], ACT.Copy)
                last.then_inc(mlp_act, 1)

            def reduce(t, u, s):
                n, size, _ = SLOTS[s]
                act.wait_ge(mult_done, NS * t + s + 1)
                for m in range(share(size), size):
                    x = prod[:, s % PRING, m * D:(m + 1) * D]
                    last = nc.scalar.activation(x, x, ACT.Copy, accum_out=z[:, u, n + m:n + m + 1])
                last.then_inc(act_reduced, 1)

            cast_k(0)
            cast_k(1)
            cast(0, 0, 0, 0, start=True)
            cast(1, 0, 0, 1, start=True)
            evacuate_quad(0, 0)
            cast(2, 0, 0, 2)
            evacuate_quad(1, 1)
            cast(3, 0, 0, 3)

            def body(b, first, last):
                for u in range(2):
                    t = 2 * b + u
                    more = not (last and u == 1)
                    for s in range(NS):
                        if s in TR_AT:
                            ahead, q = TR_AT[s]
                            if more or not ahead:
                                evacuate_quad(QUADS * (t + ahead) + q, q)
                        if first and u == 0 and s + 2 < NS:
                            cast_k(s + 2)
                        if s in CAST_AT:
                            ahead, q = CAST_AT[s]
                            if more or not ahead:
                                bb, uu = (b, u) if not ahead else (b, 1) if u == 0 else (b + 1, 0)
                                cast(QUADS * (t + ahead) + q, bb, uu, q)
                        if s in EVAC_AT and u == 0 and not first:
                            mlp_evacuate(b, EVAC_AT[s])
                        if u == 1 and s == 6:
                            if not first:
                                act.wait_ge(y_out, 16 * b)
                            if first:
                                act.wait_ge(k_done, NS)
                                act.wait_ge(weights_in, 5 * 16)
                            mlp_evacuate(b, 5)
                        if s == 0 and not (first):
                            act.wait_ge(mlp_pe, z_read(b - 1, u))
                        reduce(t, u, s)

            bodies(act, body)
            for batch in range(5):
                mlp_evacuate(BODIES, batch)

        @block.vector
        def _(dve):
            def low_k(c):
                n, size, _ = SLOTS[c]
                cols = slice(n * D, (n + size) * D)
                dve.wait_ge(kh_done, c + 1)
                nc.vector.tensor_tensor(kst[D:P, cols], raw[:, c % 2, 0:size * D], kst[0:D, cols].bitcast(F32),
                                        ALU.subtract).then_inc(k_done, 1)

            def multiply(t, u, s, first):
                n, size, segs = SLOTS[s]
                dve.wait_ge(t_ready, NS * t + s + 1)
                if not (first and u == 0 and s < PRING):
                    dve.wait_ge(act_reduced, NS * t + s - PRING + 1)
                    dve.wait_ge(dve_reduced, NS * t + s - PRING + 1)
                for i, j, m, w in segs:
                    c = (m - n) * D
                    last = nc.vector.tensor_tensor(prod[:, s % PRING, c:c + w * D], T[:, s % 2, c:c + w * D],
                                                   E[:, u, j:j + w, :].rearrange("p f h -> p (f h)"), ALU.mult)
                last.then_inc(mult_done, 1)

            def reduce(t, u, s):
                n, size, _ = SLOTS[s]
                k = share(size)
                dve.wait_ge(mult_done, NS * t + s + 1)
                nc.vector.tensor_reduce(z[:, u, n:n + k], prod[:, s % PRING, 0:k * D].rearrange("p (n h) -> p n h", h=D),
                                        AX_X, ALU.add).then_inc(dve_reduced, 1)

            low_k(0)
            low_k(1)
            dve.wait_ge(ident_1, 1)
            nc.vector.tensor_copy(identr[:, :], ident[:, :]).then_inc(identr_done, 1)

            def body(b, first, last):
                for u in range(2):
                    t = 2 * b + u
                    for s in range(NS):
                        if s == 0:
                            for q in range(QUADS):
                                dve.wait_ge(gathered[u][q], 16 * QF * (b + 1))
                        if first and u == 0 and s + 2 < NS:
                            low_k(s + 2)
                        multiply(t, u, s, first)
                        if s == 1 and not first:
                            dve.wait_ge(mlp_pe, z_read(b - 1, u))
                        if s >= 1:
                            reduce(t, u, s - 1)
                    reduce(t, u, NS - 1)

            bodies(dve, body)

        @block.tensor
        def _(pe):
            def transpose_quad(Q, q):
                pe.wait_ge(low_done, Q + 1)
                if not (isinstance(Q, int) and Q == 0):
                    pe.wait_ge(a_done, Q)
                for f in range(min(QF, NF - 1 - QF * q)):
                    last = nc.tensor.transpose(psE[:, f * P:(f + 1) * P].bitcast(F32R),
                                               nat[:, q % 2, f, :, :].rearrange("p a h -> p (a h)"), identr[:, :])
                last.then_inc(e_transposed, 1)

            def products(t, s, first):
                n, size, segs = SLOTS[s]
                if first:
                    pe.wait_ge(k_done, s + 1)
                for q in range(QUADS):
                    if first_use[q] == s:
                        pe.wait_ge(b_done[q % ERING], 32 * (QUADS // ERING * t + q // ERING + 1))
                if not (first and s < 2):
                    pe.wait_ge(mult_done, NS * t + s - 1)
                for i, j, m, w in segs:
                    while w:
                        c = m - n
                        k = min(w, HB - c % HB)
                        o = T[:, s % 2, c * D:(c + k) * D]
                        rhs = kst[:, m * D:(m + k) * D]
                        nc.tensor.matmul(o, eA[:, i // QF % ERING, i % QF, :], rhs, start=True, stop=False)
                        last = nc.tensor.matmul(o, eB[:, i // QF % ERING, i % QF, :], rhs, start=False, stop=True)
                        m += k
                        w -= k
                last.then_inc(t_ready, 1)

            def transpose_z(t, u, b, batch):
                pe.wait_ge(dve_reduced, NS * (t + 1))
                pe.wait_ge(act_reduced, NS * (t + 1))
                pe.wait_ge(dense_in[u], 16 * (b + 1 if u == 0 else b))
                o = ordinal(b, batch)
                if not (isinstance(o, int) and o == 0):
                    pe.wait_ge(mlp_act, o)
                for k in range(KC):
                    last = nc.tensor.transpose(psM[:, 0, k * P:(k + 1) * P], z[:, u, k * P:(k + 1) * P], ident[:, :])
                last.then_inc(mlp_pe, 1)

            def layer(o, w, src, m, half, blocks):
                for k in range(half * blocks // 2, (half + 1) * blocks // 2):
                    last = nc.tensor.matmul(o, w[:, k, m * P:(m + 1) * P], src[:, k, :], start=(k == 0), stop=(k == blocks - 1))
                return last

            def layer1(b, m, half):
                if m == 0 and half == 0:
                    pe.wait_ge(mlp_act, ordinal(b, 1))
                last = layer(psM[:, 1 - m // 2, (m % 2) * PB:(m % 2 + 1) * PB], w1, zT, m, half, KC)
                if m % 2 and half:
                    last.then_inc(mlp_pe, 1)

            def layer2(b, m, half):
                if m == 0 and half == 0:
                    pe.wait_ge(mlp_act, ordinal(b, 3))
                last = layer(psM[:, 1, m * PB:(m + 1) * PB], w2, h1T, m, half, M1)
                if m == M2 - 1 and half:
                    last.then_inc(mlp_pe, 1)

            def layer3(b):
                pe.wait_ge(mlp_act, ordinal(b, 4))
                for k in range(M2):
                    last = nc.tensor.matmul(psM[0:1, 0, 0:PB], w3[:, k:k + 1], h2T[:, k, :], start=(k == 0), stop=(k == M2 - 1))
                last.then_inc(mlp_pe, 1)

            pe.wait_ge(identr_done, 1)
            transpose_quad(0, 0)
            transpose_quad(1, 1)

            def body(b, first, last):
                for u in range(2):
                    t = 2 * b + u
                    more = not (last and u == 1)
                    for s in range(NS):
                        products(t, s, first and u == 0)
                        if s in TR_AT:
                            ahead, q = TR_AT[s]
                            if more or not ahead:
                                transpose_quad(QUADS * (t + ahead) + q, q)
                        if u == 0 and not first:
                            if s == Z_AT:
                                transpose_z(t - 1, 1, b, 0)
                            if s in L1_AT:
                                layer1(b, *L1_AT[s])
                            if s in L2_AT:
                                layer2(b, *L2_AT[s])
                            if s == L3_AT:
                                layer3(b)
                        if u == 1 and s == Z_AT:
                            if first:
                                pe.wait_ge(weights_in, 5 * 16)
                            transpose_z(t - 1, 0, b, 5)

            bodies(pe, body)
            transpose_z(TILES - 1, 1, BODIES, 0)
            for m in range(M1):
                for half in range(2):
                    layer1(BODIES, m, half)
            for m in range(M2):
                for half in range(2):
                    layer2(BODIES, m, half)
            layer3(BODIES)


def kernel(**inputs):
    import numpy as np
    import concourse.bacc as bacc
    from concourse.bass_utils import run_bass_kernel_spmd

    nc = bacc.Bacc("TRN2", target_bir_lowering=False, num_devices=1)
    arrays = {}

    def given(name, a):
        a = np.ascontiguousarray(a)
        arrays[name] = a
        return nc.dram_tensor(name, a.shape, mybir.dt.from_np(a.dtype), kind="ExternalInput").ap()

    fields = inputs["ids"].shape[1]
    args = [given(n, inputs[n]) for n in ("dense_ctx", "ids")]
    args.append([given(f"tbl_{f}", inputs[f"tbl_{f}"]) for f in range(fields)])
    args += [given("W_top1", inputs["W_top1"]), given("b_top1", np.asarray(inputs["b_top1"]).reshape(-1, P).T),
             given("W_top2", inputs["W_top2"]), given("b_top2", np.asarray(inputs["b_top2"]).reshape(-1, P).T),
             given("W_top3", np.asarray(inputs["W_top3"]).reshape(-1, P).T)]
    k = np.asarray(inputs["L0_rec_kernel"])
    args.append(given("K_T", k.transpose(2, 1, 0).reshape(k.shape[2], -1)))
    batch = inputs["ids"].shape[0]
    out = nc.dram_tensor("y_out_dram", (1, batch), F32, kind="ExternalOutput").ap()
    dlrm_tower(nc, *args, out)
    r = run_bass_kernel_spmd(nc, [arrays], core_ids=[0])
    return r.results[0]["y_out_dram"].reshape(batch, 1)
```

```python
from contextlib import ExitStack

import concourse.bass as bass
from concourse import mybir

ALU = mybir.AluOpType
ACT = mybir.ActivationFunctionType
AX_X = mybir.AxisListType.X
F32 = mybir.dt.float32
F32R = mybir.dt.float32r
I32 = mybir.dt.int32
U32 = mybir.dt.uint32

P = 128
BANK = 512
QF = 4
SLOT = 16
PRING = 4
ACT_PAIRS = 8
FOLD = 8
K_PIECES = 16
KRING = 4


def first_pair(i, fields):
    return i * (fields - 1) - i * (i - 1) // 2


def plan(fields):
    pairs = fields * (fields - 1) // 2
    half = SLOT // 2
    sizes = [SLOT] * (pairs // SLOT - 1) + [half, half]
    assert sum(sizes) == pairs and len(sizes) % PRING == 0
    slots, n = [], 0
    for size in sizes:
        segs, m = [], n
        while m < n + size:
            i = max(r for r in range(fields - 1) if first_pair(r, fields) <= m)
            w = min(first_pair(i + 1, fields), n + size) - m
            segs.append((i, i + 1 + m - first_pair(i, fields), m, w))
            m += w
        slots.append((n, size, segs))
        n += size
    return slots


def dlrm_tower(nc, dense, ids, tables, W1, b1, W2, b2, W3, KT, out):
    B, DC = dense.shape
    NF = len(tables)
    D = tables[0].shape[1]
    H1, H2 = W2.shape
    TILES = B // P
    BODIES = TILES // 2
    NP = NF * (NF - 1) // 2
    QUADS = NF // QF
    CP = NP // K_PIECES
    KC = W1.shape[0] // P
    M1, M2 = H1 // P, H2 // P
    PB = 2 * P
    HB = BANK // D
    SLOTS = plan(NF)
    NS = len(SLOTS)
    assert NP + DC == KC * P and M1 == KC and D == P // 2 and TILES % 2 == 0

    first_use = [min(s for s, (_, _, g) in enumerate(SLOTS) if any(x[0] // QF == q for x in g)) for q in range(QUADS)]
    last_use = [max(s for s, (_, _, g) in enumerate(SLOTS) if any(x[0] // QF == q for x in g)) for q in range(QUADS)]
    ERING = 4
    TR_AT = {1: (0, 2), 3: (0, 3), 8: (0, 4), 14: (0, 5), 20: (0, 6), 24: (0, 7), 27: (1, 0), 30: (1, 1)}
    CAST_AT = {4: (0, 4), 10: (0, 5), 16: (0, 6), 20: (0, 7), 23: (1, 0), 26: (1, 1), 29: (1, 2), 31: (1, 3)}
    for s, (ahead, q) in TR_AT.items():
        before = q + QUADS * ahead - ERING
        assert before < 0 or s >= last_use[before]
        assert s < first_use[q] + NS * ahead
    SUMMED = [s for s in range(NS) if s % PRING == 0 and SLOTS[s][1] == SLOT]
    SHARED = [s for s in range(NS) if s not in SUMMED]

    def before(kind, s):
        return sum(k < s for k in kind) if s >= 0 else sum(k < s + NS for k in kind) - len(kind)

    REDUCE_AT = {}
    for k in SHARED:
        at = k + 1
        if at in SUMMED:
            at += 1
        REDUCE_AT.setdefault(min(at, NS), []).append(k)

    Z_ODD_AT = (0, 4)
    L1_AT = {at: (n // 2, n % 2) for n, at in enumerate([(0, s) for s in (8, 9, 12, 13, 16, 17, 20, 21)])}
    L2_AT = {at: (n // 2, n % 2) for n, at in enumerate([(1, s) for s in (0, 1, 4, 5)])}
    L3_AT = (1, 9)
    Z_EVEN_AT = (1, 13)
    EVAC_AT = {(0, 6): 0, (0, 14): 1, (0, 22): 2, (1, 6): 3, (1, 11): 4, (1, 15): 5}
    BATCHES = 6
    assert len(L1_AT) == 2 * M1 and len(L2_AT) == 2 * M2

    ctx = ExitStack()
    with ctx:
        def sb(name, shape, dt):
            return ctx.enter_context(nc.sbuf_tensor(name, shape, dt))

        def sem(name):
            return ctx.enter_context(nc.semaphore(name))

        kst = sb("kst", [P, NP * D], F32R)
        E = sb("E", [P, 2, NF, D], F32)
        nat = sb("nat", [P, 2, QF, 2, D], F32R)
        eA = sb("eA", [P, ERING, QF, P], F32R)
        eB = sb("eB", [P, ERING, QF, P], F32R)
        prod = sb("prod", [P, PRING, SLOT * D], F32)
        z = sb("z", [P, 2, KC * P], F32)
        mlp = sb("mlp", [P, (KC + M1 + M2) * PB + KC * H1 + M1 * H2], F32)
        mlp_at = 0

        def part(blocks, width):
            nonlocal mlp_at
            mlp_at += blocks * width
            return mlp[:, mlp_at - blocks * width:mlp_at].rearrange("p (k c) -> p k c", k=blocks)

        zT, h1T, h2T, w1, w2 = part(KC, PB), part(M1, PB), part(M2, PB), part(KC, H1), part(M1, H2)
        raw = [place[:, k * CP * D:(k + 1) * CP * D]
               for place in (prod[0:D, :, :].rearrange("p a b -> p (a b)"), mlp[0:D, :]) for k in range(KRING // 2)]
        w3 = sb("w3", [P, M2], F32)
        b1c = sb("b1c", [P, M1], F32)
        b2c = sb("b2c", [P, M2], F32)
        ident = sb("ident", [P, P], F32)
        identr = sb("identr", [P, P], F32R)
        idx = sb("idx", [P, 2, NF], I32)
        y = sb("y", [1, PB], F32)

        T = ctx.enter_context(nc.psum_tensor("T", [P, 2, SLOT * D], F32))
        psE = ctx.enter_context(nc.psum_tensor("psE", [P, BANK], F32))
        psZ = ctx.enter_context(nc.psum_tensor("psZ", [P, SLOT, FOLD], F32))
        psM = ctx.enter_context(nc.psum_tensor("psM", [P, 2, BANK], F32))

        idx_in = [sem(f"idx_in{u}") for u in range(2)]
        gathered = [[sem(f"gathered{u}_{q}") for q in range(QUADS)] for u in range(2)]
        dense_in = [sem(f"dense_in{u}") for u in range(2)]
        weights_in = sem("weights_in")
        k_in = [sem(f"k_in{r}") for r in range(KRING)]
        kh_done = sem("kh_done")
        k_done = sem("k_done")
        ident_0 = sem("ident_0")
        ident_1 = sem("ident_1")
        identr_done = sem("identr_done")
        cast_done = sem("cast_done")
        low_done = sem("low_done")
        e_transposed = sem("e_transposed")
        a_done = sem("a_done")
        b_done = [sem(f"b_done{r}") for r in range(ERING)]
        t_ready = sem("t_ready")
        mult_done = sem("mult_done")
        dve_reduced = sem("dve_reduced")
        act_reduced = sem("act_reduced")
        summed = sem("summed")
        folded = sem("folded")
        mlp_pe = sem("mlp_pe")
        mlp_act = sem("mlp_act")
        y_out = sem("y_out")

        def share(size):
            return size - ACT_PAIRS * size // SLOT

        def bodies(eng, body):
            body(0, True, False)
            with eng.Fori(1, BODIES - 1) as b:
                body(b, False, False)
            body(BODIES - 1, False, True)

        def ordinal(b, batch):
            return (b - 1) * BATCHES + 1 + batch

        def z_read(b, u):
            return ordinal(b, 5) + 1 if u == 0 else ordinal(b + 1, 0) + 1

        block = ctx.enter_context(nc.Block())

        @block.sync
        def _(sp):
            def load_k(c, r):
                sp.dma_start(raw[r], KT[:, bass.ts(c, CP * D)]).then_inc(k_in[r], 16)

            def load_idx(t, u):
                sp.dma_start(idx[:, u, :], ids[bass.ts(t, P), :]).then_inc(idx_in[u], 16)

            def load_dense(t, u):
                sp.dma_start(z[:, u, NP:NP + DC], dense[bass.ts(t, P), :]).then_inc(dense_in[u], 16)

            def swap_halves(Q, r):
                sp.wait_ge(a_done, Q + 1)
                sp.dma_start(eB[0:D, r].bitcast(F32), eA[D:P, r].bitcast(F32)).then_inc(b_done[r], 16)
                sp.dma_start(eB[D:P, r].bitcast(F32), eA[0:D, r].bitcast(F32)).then_inc(b_done[r], 16)

            def store_y(b):
                sp.wait_ge(mlp_act, ordinal(b, 4) + 1)
                sp.dma_start(out[:, bass.ts(b - 1, PB)], y[:, :]).then_inc(y_out, 16)

            load_idx(0, 0)
            for r in range(KRING):
                load_k(r, r)
            load_idx(1, 1)
            with sp.Fori(1, K_PIECES // KRING) as g:
                for r in range(KRING):
                    sp.wait_ge(k_done, KRING * (g - 1) + r + 1)
                    load_k(KRING * g + r, r)
            load_dense(0, 0)
            load_dense(1, 1)
            swap_halves(0, 0)
            swap_halves(1, 1)

            def body(b, first, last):
                for u in range(2):
                    t = 2 * b + u
                    for s in range(NS):
                        if first and u == 0:
                            if s == 2:
                                sp.wait_ge(k_done, K_PIECES)
                                sp.dma_start(w1[:, :, :], W1.rearrange("(k p) m -> p k m", p=P)).then_inc(weights_in, 16)
                                sp.dma_start(w2[:, :, :], W2.rearrange("(k p) m -> p k m", p=P)).then_inc(weights_in, 16)
                                sp.dma_start(w3[:, :], W3).then_inc(weights_in, 16)
                                sp.dma_start(b1c[:, :], b1).then_inc(weights_in, 16)
                                sp.dma_start(b2c[:, :], b2).then_inc(weights_in, 16)
                        if s == (12, 30)[u] and not (first and u == 0) and not (last and u == 1):
                            sp.wait_ge(mlp_pe, z_read(b - 1 + u, 1 - u))
                            load_dense(t + 1, 1 - u)
                        if s == 26 and not last:
                            sp.wait_ge(mult_done, NS * t + 1)
                            load_idx(t + 2, u)
                        if s in TR_AT:
                            ahead, q = TR_AT[s]
                            if not (last and u == 1 and ahead):
                                swap_halves(QUADS * (t + ahead) + q, q % ERING)
                        if u == 1 and s == 12 and not first:
                            store_y(b)

            bodies(sp, body)
            store_y(BODIES)
            sp.wait_ge(y_out, 16 * BODIES)

        @block.gpsimd
        def _(pool):
            def gather(b, u, q):
                for f in range(QF * q, QF * q + QF):
                    nc.gpsimd.indirect_dma_start(
                        out=E[:, u, f, :], out_offset=None, in_=tables[f],
                        in_offset=bass.IndirectOffsetOnAxis(ap=idx[:, u, f:f + 1].bitcast(U32), axis=0),
                    ).then_inc(gathered[u][q], 16)

            def low(Q, u, q):
                pool.wait_ge(cast_done, Q + 1)
                nc.gpsimd.tensor_tensor(nat[:, q % 2, :, 1, :], E[:, u, QF * q:QF * q + QF, :],
                                        nat[:, q % 2, :, 0, :].bitcast(F32), ALU.subtract).then_inc(low_done, 1)

            nc.gpsimd.memset(ident[:, :], 0.0).then_inc(ident_0, 1)
            pool.wait_ge(idx_in[0], 16)
            gather(0, 0, 0)
            pool.wait_ge(ident_0, 1)
            nc.gpsimd.affine_select(out=ident[:, :], in_=ident[:, :], compare_op=ALU.not_equal, fill=1.0,
                                    base=0, pattern=[[-1, P]], channel_multiplier=1).then_inc(ident_1, 1)
            for q in range(1, QUADS):
                gather(0, 0, q)
                if q == 3:
                    low(0, 0, 0)
                if q == 4:
                    low(1, 0, 1)

            def body(b, first, last):
                for u in range(2):
                    t = 2 * b + u
                    more = not (last and u == 1)

                    def ahead(q):
                        if more:
                            gather(b, 1 - u, q)
                    low(QUADS * t + 2, u, 2)
                    if more:
                        pool.wait_ge(idx_in[1 - u], 16 * (b + 1 + u))
                        if not (first and u == 0):
                            pool.wait_ge(mult_done, NS * t)
                    low(QUADS * t + 3, u, 3)
                    for q in range(4, QUADS):
                        ahead(2 * (q - 4))
                        ahead(2 * (q - 4) + 1)
                        low(QUADS * t + q, u, q)
                    if more:
                        low(QUADS * (t + 1), 1 - u, 0)
                        low(QUADS * (t + 1) + 1, 1 - u, 1)

            bodies(pool, body)

        @block.scalar
        def _(act):
            def cast_k(start, end):
                with act.Fori(start, end) as g:
                    for r in range(KRING):
                        act.wait_ge(k_in[r], 16 * g + 16)
                        nc.scalar.activation(kst[0:D, bass.ts(KRING * g + r, CP * D)], raw[r],
                                             ACT.Copy).then_inc(kh_done, 1)

            def cast(Q, b, u, q, start=False):
                act.wait_ge(gathered[u][q], 16 * QF * (b + 1))
                if not start:
                    act.wait_ge(e_transposed, Q - 1)
                nc.scalar.activation(nat[:, q % 2, :, 0, :], E[:, u, QF * q:QF * q + QF, :],
                                     ACT.Copy).then_inc(cast_done, 1)

            def evacuate_quad(Q, q):
                act.wait_ge(e_transposed, Q + 1)
                fields = min(QF, NF - 1 - QF * q)
                nc.scalar.activation(eA[:, q % ERING, 0:fields, :],
                                     psE[:, 0:fields * P].rearrange("p (f b) -> p f b", b=P),
                                     ACT.Copy).then_inc(a_done, 1)

            def mlp_evacuate(b, batch):
                act.wait_ge(mlp_pe, ordinal(b, batch) + 1)
                bank = psM[:, 1 if batch in (1, 3) else 0, :]
                halves = bank.rearrange("p (m b) -> p m b", m=2)
                if batch in (0, 5):
                    u = 1 if batch == 0 else 0
                    last = nc.scalar.activation(zT[:, :, u * P:(u + 1) * P],
                                                bank.rearrange("p (k b) -> p k b", k=KC), ACT.Copy)
                elif batch in (1, 2):
                    for m in range(2):
                        mm = 2 * (batch - 1) + m
                        last = nc.scalar.activation(h1T[:, mm, :], halves[:, m, :], ACT.Relu, bias=b1c[:, mm:mm + 1])
                elif batch == 3:
                    for m in range(M2):
                        last = nc.scalar.activation(h2T[:, m, :], halves[:, m, :], ACT.Relu, bias=b2c[:, m:m + 1])
                else:
                    last = nc.scalar.activation(y[:, :], bank[0:1, 0:PB], ACT.Copy)
                last.then_inc(mlp_act, 1)

            def reduce(t, u, s):
                n, size, _ = SLOTS[s]
                act.wait_ge(mult_done, NS * t + s + 1)
                for m in range(share(size), size):
                    x = prod[:, s % PRING, m * D:(m + 1) * D]
                    last = nc.scalar.activation(x, x, ACT.Copy, accum_out=z[:, u, n + m:n + m + 1])
                last.then_inc(act_reduced, 1)

            cast_k(0, 1)
            cast(0, 0, 0, 0, start=True)
            cast(1, 0, 0, 1, start=True)
            cast_k(1, 2)
            evacuate_quad(0, 0)
            cast(2, 0, 0, 2)
            evacuate_quad(1, 1)
            cast(3, 0, 0, 3)
            cast_k(2, K_PIECES // KRING)

            def body(b, first, last):
                for u in range(2):
                    t = 2 * b + u
                    more = not (last and u == 1)
                    for s in range(NS):
                        if s in TR_AT:
                            ahead, q = TR_AT[s]
                            if more or not ahead:
                                evacuate_quad(QUADS * (t + ahead) + q, q)
                        if s in CAST_AT:
                            ahead, q = CAST_AT[s]
                            if more or not ahead:
                                bb, uu = (b, u) if not ahead else (b, 1) if u == 0 else (b + 1, 0)
                                cast(QUADS * (t + ahead) + q, bb, uu, q)
                        batch = EVAC_AT.get((u, s))
                        if first and batch == 5:
                            act.wait_ge(weights_in, 5 * 16)
                        if batch is not None and (batch == 5 or not first):
                            mlp_evacuate(b, batch)
                        if u == 1 and s == 31 and not first:
                            act.wait_ge(y_out, 16 * b)
                        if s == 0 and not (first):
                            act.wait_ge(mlp_pe, z_read(b - 1, u))
                        if s in SHARED:
                            reduce(t, u, s)

            bodies(act, body)
            for batch in range(5):
                mlp_evacuate(BODIES, batch)

        @block.vector
        def _(dve):
            def low_k(c, r):
                cols = bass.ts(c, CP * D)
                dve.wait_ge(kh_done, c + 1)
                nc.vector.tensor_tensor(kst[D:P, cols], raw[r], kst[0:D, cols].bitcast(F32),
                                        ALU.subtract).then_inc(k_done, 1)

            def multiply(t, u, s, first):
                n, size, segs = SLOTS[s]
                dve.wait_ge(t_ready, NS * t + s + 1)
                if first and u == 0 and s < PRING:
                    dve.wait_ge(k_done, K_PIECES)
                elif (s - PRING) % NS in SUMMED:
                    dve.wait_ge(summed, len(SUMMED) * t + before(SUMMED, s - PRING) + 1)
                else:
                    count = len(SHARED) * t + before(SHARED, s - PRING) + 1
                    dve.wait_ge(act_reduced, count)
                    dve.wait_ge(dve_reduced, count)
                for i, j, m, w in segs:
                    c = (m - n) * D
                    last = nc.vector.tensor_tensor(prod[:, s % PRING, c:c + w * D], T[:, s % 2, c:c + w * D],
                                                   E[:, u, j:j + w, :].rearrange("p f h -> p (f h)"), ALU.mult)
                last.then_inc(mult_done, 1)

            def reduce(t, u, s):
                n, size, _ = SLOTS[s]
                k = share(size)
                dve.wait_ge(mult_done, NS * t + s + 1)
                nc.vector.tensor_reduce(z[:, u, n:n + k], prod[:, s % PRING, 0:k * D].rearrange("p (n h) -> p n h", h=D),
                                        AX_X, ALU.add).then_inc(dve_reduced, 1)

            def fold(t, u, s):
                n, size, _ = SLOTS[s]
                dve.wait_ge(summed, len(SUMMED) * t + before(SUMMED, s) + 1)
                nc.vector.tensor_reduce(z[:, u, n:n + size], psZ[:, :, :], AX_X, ALU.add).then_inc(folded, 1)

            for r in range(KRING):
                low_k(r, r)
            dve.wait_ge(ident_1, 1)
            nc.vector.tensor_copy(identr[:, :], ident[:, :]).then_inc(identr_done, 1)
            with dve.Fori(1, K_PIECES // KRING) as g:
                for r in range(KRING):
                    low_k(KRING * g + r, r)

            def body(b, first, last):
                for u in range(2):
                    t = 2 * b + u
                    for s in range(NS):
                        if s == 0:
                            for q in range(QUADS):
                                dve.wait_ge(gathered[u][q], 16 * QF * (b + 1))
                        multiply(t, u, s, first)
                        if s == 1 and not first:
                            dve.wait_ge(mlp_pe, z_read(b - 1, u))
                        if s - PRING in SUMMED:
                            fold(t, u, s - PRING)
                        for k in REDUCE_AT.get(s, []):
                            reduce(t, u, k)
                    fold(t, u, NS - PRING)
                    for k in REDUCE_AT[NS]:
                        reduce(t, u, k)

            bodies(dve, body)

        @block.tensor
        def _(pe):
            def transpose_quad(Q, q):
                pe.wait_ge(low_done, Q + 1)
                if not (isinstance(Q, int) and Q == 0):
                    pe.wait_ge(a_done, Q)
                for f in range(min(QF, NF - 1 - QF * q)):
                    last = nc.tensor.transpose(psE[:, f * P:(f + 1) * P].bitcast(F32R),
                                               nat[:, q % 2, f, :, :].rearrange("p a h -> p (a h)"), identr[:, :])
                last.then_inc(e_transposed, 1)

            def products(t, s, first):
                n, size, segs = SLOTS[s]
                if first and s == 0:
                    pe.wait_ge(k_done, K_PIECES)
                for q in range(QUADS):
                    if first_use[q] == s:
                        pe.wait_ge(b_done[q % ERING], 32 * (QUADS // ERING * t + q // ERING + 1))
                if not (first and s < 2):
                    pe.wait_ge(mult_done, NS * t + s - 1)
                for i, j, m, w in segs:
                    while w:
                        c = m - n
                        k = min(w, HB - c % HB)
                        o = T[:, s % 2, c * D:(c + k) * D]
                        rhs = kst[:, m * D:(m + k) * D]
                        nc.tensor.matmul(o, eA[:, i // QF % ERING, i % QF, :], rhs, start=True, stop=False)
                        last = nc.tensor.matmul(o, eB[:, i // QF % ERING, i % QF, :], rhs, start=False, stop=True)
                        m += k
                        w -= k
                last.then_inc(t_ready, 1)

            def sum_products(t, s, half):
                if half == 0:
                    pe.wait_ge(mult_done, NS * t + s + 1)
                    if not (isinstance(t, int) and t == 0 and s == SUMMED[0]):
                        pe.wait_ge(folded, len(SUMMED) * t + before(SUMMED, s))
                steps = D // FOLD
                for k in range(half * steps // 2, (half + 1) * steps // 2):
                    x = prod[:, s % PRING, :].rearrange("p (n h) -> p n h", h=D)[:, :, k * FOLD:(k + 1) * FOLD]
                    last = nc.tensor.matmul(psZ[:, :, :], ident[:, :], x, start=(k == 0), stop=(k == steps - 1))
                if half:
                    last.then_inc(summed, 1)

            def transpose_z(t, u, b, batch):
                pe.wait_ge(dve_reduced, len(SHARED) * (t + 1))
                pe.wait_ge(act_reduced, len(SHARED) * (t + 1))
                pe.wait_ge(folded, len(SUMMED) * (t + 1))
                pe.wait_ge(dense_in[u], 16 * (b + 1 if u == 0 else b))
                o = ordinal(b, batch)
                if not (isinstance(o, int) and o == 0):
                    pe.wait_ge(mlp_act, o)
                for k in range(KC):
                    last = nc.tensor.transpose(psM[:, 0, k * P:(k + 1) * P], z[:, u, k * P:(k + 1) * P], ident[:, :])
                last.then_inc(mlp_pe, 1)

            def layer(o, w, src, m, half, blocks):
                for k in range(half * blocks // 2, (half + 1) * blocks // 2):
                    last = nc.tensor.matmul(o, w[:, k, m * P:(m + 1) * P], src[:, k, :], start=(k == 0), stop=(k == blocks - 1))
                return last

            def layer1(b, m, half):
                if m == 0 and half == 0:
                    pe.wait_ge(mlp_act, ordinal(b, 1))
                last = layer(psM[:, 1 - m // 2, (m % 2) * PB:(m % 2 + 1) * PB], w1, zT, m, half, KC)
                if m % 2 and half:
                    last.then_inc(mlp_pe, 1)

            def layer2(b, m, half):
                if m == 0 and half == 0:
                    pe.wait_ge(mlp_act, ordinal(b, 3))
                last = layer(psM[:, 1, m * PB:(m + 1) * PB], w2, h1T, m, half, M1)
                if m == M2 - 1 and half:
                    last.then_inc(mlp_pe, 1)

            def layer3(b):
                pe.wait_ge(mlp_act, ordinal(b, 4))
                for k in range(M2):
                    last = nc.tensor.matmul(psM[0:1, 0, 0:PB], w3[:, k:k + 1], h2T[:, k, :], start=(k == 0), stop=(k == M2 - 1))
                last.then_inc(mlp_pe, 1)

            pe.wait_ge(identr_done, 1)
            transpose_quad(0, 0)
            transpose_quad(1, 1)

            def body(b, first, last):
                for u in range(2):
                    t = 2 * b + u
                    more = not (last and u == 1)
                    for s in range(NS):
                        products(t, s, first and u == 0)
                        for half in range(2):
                            if s - 2 - half in SUMMED:
                                sum_products(t, s - 2 - half, half)
                        if s in TR_AT:
                            ahead, q = TR_AT[s]
                            if more or not ahead:
                                transpose_quad(QUADS * (t + ahead) + q, q)
                        at = (u, s)
                        if not first:
                            if at == Z_ODD_AT:
                                transpose_z(t - 1, 1, b, 0)
                            if at in L1_AT:
                                layer1(b, *L1_AT[at])
                            if at in L2_AT:
                                layer2(b, *L2_AT[at])
                            if at == L3_AT:
                                layer3(b)
                        if at == Z_EVEN_AT:
                            if first:
                                pe.wait_ge(weights_in, 5 * 16)
                            transpose_z(t - 1, 0, b, 5)

            bodies(pe, body)
            transpose_z(TILES - 1, 1, BODIES, 0)
            for m in range(M1):
                for half in range(2):
                    layer1(BODIES, m, half)
            for m in range(M2):
                for half in range(2):
                    layer2(BODIES, m, half)
            layer3(BODIES)


def kernel(**inputs):
    import numpy as np
    import concourse.bacc as bacc
    from concourse.bass_utils import run_bass_kernel_spmd

    nc = bacc.Bacc("TRN2", target_bir_lowering=False, num_devices=1)
    arrays = {}

    def given(name, a):
        a = np.ascontiguousarray(a)
        arrays[name] = a
        return nc.dram_tensor(name, a.shape, mybir.dt.from_np(a.dtype), kind="ExternalInput").ap()

    fields = inputs["ids"].shape[1]
    args = [given(n, inputs[n]) for n in ("dense_ctx", "ids")]
    args.append([given(f"tbl_{f}", inputs[f"tbl_{f}"]) for f in range(fields)])
    args += [given("W_top1", inputs["W_top1"]), given("b_top1", np.asarray(inputs["b_top1"]).reshape(-1, P).T),
             given("W_top2", inputs["W_top2"]), given("b_top2", np.asarray(inputs["b_top2"]).reshape(-1, P).T),
             given("W_top3", np.asarray(inputs["W_top3"]).reshape(-1, P).T)]
    k = np.asarray(inputs["L0_rec_kernel"])
    args.append(given("K_T", k.transpose(2, 1, 0).reshape(k.shape[2], -1)))
    batch = inputs["ids"].shape[0]
    out = nc.dram_tensor("y_out_dram", (1, batch), F32, kind="ExternalOutput").ap()
    dlrm_tower(nc, *args, out)
    r = run_bass_kernel_spmd(nc, [arrays], core_ids=[0])
    return r.results[0]["y_out_dram"].reshape(batch, 1)
```

```python
from contextlib import ExitStack

import concourse.bass as bass
from concourse import mybir

ALU = mybir.AluOpType
ACT = mybir.ActivationFunctionType
AX_X = mybir.AxisListType.X
F32 = mybir.dt.float32
F32R = mybir.dt.float32r
I32 = mybir.dt.int32
U32 = mybir.dt.uint32

P = 128
BANK = 512
QF = 4
SLOT = 16
EVAC_LEAD = 1
LOW_AFTER = (1, 2, 3, 5)
WITHIN_AT = {7: 0, 18: 2, 26: 4, 31: 6, 32: 6}
T_RING = 3
SHARED_RING = 3
SUMMED_RING = 2
ACT_PAIRS = 8
K_LEAD, K_STEP = 11, 2
K_AHEAD = 3
K_GPSIMD, K_GPSIMD_AT = 28, 14.96
MLP_SLOTS = ((0, 5), (0, 10), (0, 16), (0, 22), (0, 29), (1, 5), (1, 10), (1, 16), (1, 22))
GATHER_FROM, GATHER_STEP = 0.5, 0.85
FOLD = 8
KRING = 5


def plan(fields):
    quads = fields // QF
    kinds = [(i, j) for i in range(quads) for j in range(i + 1, quads)]
    for s, i in WITHIN_AT.items():
        kinds.insert(s, (i, None))
    slots, n = [], 0
    for i, j in kinds:
        if j is None:
            quad = [QF * i, QF * i + QF]
            crossing = [(q + a, q + b) for q in quad for a in (0, 1) for b in (2, 3)]
            beside = [(q + a, q + a + 1) for q in quad for a in (0, 2)]
            last = [s for s, x in WITHIN_AT.items() if x == i]
            pairs = crossing + beside if len(last) == 1 else crossing if len(slots) == last[0] else beside
        else:
            pairs = [(QF * i + a, QF * j + b) for a in range(QF) for b in range(QF)]
        slots.append((n, pairs, i, j))
        n += len(pairs)
    assert n == fields * (fields - 1) // 2 and len(slots) % T_RING == 0
    return slots


def runs(pairs):
    out = []
    for m, (i, _) in enumerate(pairs):
        if out and out[-1][0] == i:
            out[-1][2] += 1
        else:
            out.append([i, m, 1])
    return out


def dlrm_tower(nc, dense, ids, tables, W1, b1, W2, b2, W3, KT, out):
    B, DC = dense.shape
    NF = len(tables)
    D = tables[0].shape[1]
    H1, H2 = W2.shape
    TILES = B // P
    BODIES = TILES // 2
    NP = NF * (NF - 1) // 2
    QUADS = NF // QF
    KC = W1.shape[0] // P
    M1, M2 = H1 // P, H2 // P
    PB = 2 * P
    SLOTS = plan(NF)
    NS = len(SLOTS)
    assert NP + DC == KC * P and M1 == KC and D == P // 2 and TILES % 2 == 0

    uses = [[s for s, (_, pairs, _, _) in enumerate(SLOTS) if any(i // QF == q for i, _ in pairs)] for q in range(QUADS)]
    first_use, last_use = [min(x) for x in uses], [max(x) for x in uses]
    ERING = 4
    TR_AT = {1: (0, 2), 3: (0, 3), 8: (0, 4), 14: (0, 5), 20: (0, 6), 24: (0, 7), 27: (1, 0), 31: (1, 1)}
    CAST_AT = {4: (0, 4), 8: (0, 5), 14: (0, 6), 18: (0, 7), 21: (1, 0), 24: (1, 1), 28: (1, 2), 31: (1, 3)}
    START_CAST_AT = {0: 2, 2: 3}
    for s, (ahead, q) in TR_AT.items():
        before = q + QUADS * ahead - ERING
        assert before < 0 or s >= last_use[before]
        assert s < first_use[q] + NS * ahead
    GATHERS_AT = {}
    for q in range(QUADS):
        at = min(s for s, (_, _, i, j) in enumerate(SLOTS) if q in ((i, i + 1) if j is None else (j,)))
        GATHERS_AT.setdefault(at, []).append(q)
    WHOLE = [4, 12, 16, 20]
    HALVED = [1, 8, 24, 28, 30]
    SUMMED = sorted(WHOLE + HALVED)
    SHARED = [s for s in range(NS) if s not in SUMMED]
    assert all(len(SLOTS[s][1]) == SLOT for s in SUMMED)
    assert 2 * len(SUMMED) % SUMMED_RING == 0 and 2 * len(SHARED) % SHARED_RING == 0
    STEPS = D // FOLD

    def place(u, s):
        if s in SHARED:
            return (len(SHARED) * u + SHARED.index(s)) % SHARED_RING
        return SHARED_RING + (len(SUMMED) * u + SUMMED.index(s)) % SUMMED_RING

    def by_slot(items):
        at = {}
        for s, *item in items:
            at.setdefault(s % NS, []).append((s // NS, *item))
        return at

    SUM_AT = by_slot([(k + 3, k) for k in SUMMED])
    FOLD_AT = by_slot([(k + 4, k) for k in SUMMED])
    REDUCE_AT = by_slot([(k + 1 + (k + 1 in SUMMED), k) for k in SHARED])

    PAST = 1 + max(s for at in (SUM_AT, FOLD_AT, REDUCE_AT) for s in at if any(x[0] for x in at[s]))

    MLP = [("z", 1)] + [("layer1", m) for m in range(M1)] + [("layer2", m) for m in range(M2)] + [("layer3", 0), ("z", 0)]
    BATCHES = len(MLP)
    MLP_AT = {at: batch for batch, at in enumerate(MLP_SLOTS)}
    assert len(MLP_AT) == BATCHES and not any(s in TR_AT or s in SUM_AT for _, s in MLP_AT)

    QUAD_EVAC_AT = {s - EVAC_LEAD: x for s, x in TR_AT.items()}
    MLP_EVAC_AT = {(u, s - EVAC_LEAD): batch for (u, s), batch in MLP_AT.items()}

    def quads_before(s):
        return sum(x <= s for x in TR_AT)

    def batches_before(u, s):
        return sum(at < (u, s) for at in MLP_AT)

    ctx = ExitStack()
    with ctx:
        def sb(name, shape, dt):
            return ctx.enter_context(nc.sbuf_tensor(name, shape, dt))

        def sem(name):
            return ctx.enter_context(nc.semaphore(name))

        kst = sb("kst", [P, NP * D], F32R)
        E = sb("E", [P, 2, NF, D], F32)
        nat = sb("nat", [P, 2, QF, 2, D], F32R)
        eA = sb("eA", [P, ERING, QF, P], F32R)
        eB = sb("eB", [P, ERING, QF, P], F32R)
        prod = sb("prod", [P, SHARED_RING + SUMMED_RING, SLOT * D], F32)
        z = sb("z", [P, 2, KC * P], F32)
        mlp = sb("mlp", [P, (KC + M1 + M2) * PB + KC * H1 + M1 * H2], F32)
        mlp_at = 0

        def part(blocks, width):
            nonlocal mlp_at
            mlp_at += blocks * width
            return mlp[:, mlp_at - blocks * width:mlp_at].rearrange("p (k c) -> p k c", k=blocks)

        zT, h1T, h2T, w1, w2 = part(KC, PB), part(M1, PB), part(M2, PB), part(KC, H1), part(M1, H2)
        raw = [mlp[0:D, r * SLOT * D:(r + 1) * SLOT * D] for r in range(KRING)]
        w3 = sb("w3", [P, M2], F32)
        b1c = sb("b1c", [P, M1], F32)
        b2c = sb("b2c", [P, M2], F32)
        identr = sb("identr", [P, P], F32R)
        ident = identr[:, :].bitcast(F32)
        ident_start = z[:, 0, 0:P]
        idx = sb("idx", [P, 2, NF], I32)
        y = sb("y", [1, PB], F32)

        T = ctx.enter_context(nc.psum_tensor("T", [P, T_RING, SLOT * D], F32))
        psE = psM = ctx.enter_context(nc.psum_tensor("psE", [P, BANK], F32))
        psZ = ctx.enter_context(nc.psum_tensor("psZ", [P, SLOT, FOLD], F32))

        idx_in = [sem(f"idx_in{u}") for u in range(2)]
        gathered = [[sem(f"gathered{u}_{q}") for q in range(QUADS)] for u in range(2)]
        dense_in = [sem(f"dense_in{u}") for u in range(2)]
        weights_in = sem("weights_in")
        k_in = [sem(f"k_in{r}") for r in range(KRING)]
        kh_done = sem("kh_done")
        k_done = sem("k_done")
        k_done_pool = sem("k_done_pool")
        ident_0 = sem("ident_0")
        ident_1 = sem("ident_1")
        identr_done = sem("identr_done")
        cast_done = sem("cast_done")
        low_done = sem("low_done")
        e_transposed = sem("e_transposed")
        a_done = sem("a_done")
        b_done = [sem(f"b_done{r}") for r in range(ERING)]
        t_ready = sem("t_ready")
        mult_done = sem("mult_done")
        dve_reduced = sem("dve_reduced")
        act_reduced = sem("act_reduced")
        summed = sem("summed")
        folded = sem("folded")
        halved = sem("halved")
        mlp_pe = sem("mlp_pe")
        mlp_act = sem("mlp_act")
        y_out = sem("y_out")

        def share(size):
            return size - ACT_PAIRS * size // SLOT

        def k_cols(s):
            return slice(SLOTS[s][0] * D, (SLOTS[s][0] + len(SLOTS[s][1])) * D)

        def k_before(s, lead):
            upto = [min(NS, lead + K_STEP * x) for x in (s - 1, s)]
            return range(upto[0] if s else 0, upto[1])

        def bodies(eng, body):
            body(0, True, False)
            with eng.Fori(1, BODIES - 1) as b:
                body(b, False, False)
            body(BODIES - 1, False, True)

        def ordinal(b, batch):
            return (b - 1) * BATCHES + 1 + batch

        END = ordinal(BODIES, 0)

        def free_bank(i):
            return T[:, i // 2, i % 2 * BANK:(i % 2 + 1) * BANK]

        def z_read(b, u):
            return ordinal(b, BATCHES - 1) + 1 if u == 0 else ordinal(b + 1, 0) + 1

        block = ctx.enter_context(nc.Block())

        @block.sync
        def _(sp):
            def load_k(c):
                if c >= KRING:
                    if c - KRING < K_GPSIMD:
                        sp.wait_ge(k_done, c - KRING + 1)
                    else:
                        sp.wait_ge(k_done_pool, c - KRING - K_GPSIMD + 1)
                sp.dma_start(raw[c % KRING][:, 0:len(SLOTS[c][1]) * D], KT[:, k_cols(c)]).then_inc(k_in[c % KRING], 16)

            def load_idx(t, u):
                sp.dma_start(idx[:, u, :], ids[bass.ts(t, P), :]).then_inc(idx_in[u], 16)

            def load_dense(t, u):
                sp.dma_start(z[:, u, NP:NP + DC], dense[bass.ts(t, P), :]).then_inc(dense_in[u], 16)

            def swap_halves(Q, r):
                sp.wait_ge(a_done, Q + 1)
                sp.dma_start(eB[0:D, r].bitcast(F32), eA[D:P, r].bitcast(F32)).then_inc(b_done[r], 16)
                sp.dma_start(eB[D:P, r].bitcast(F32), eA[0:D, r].bitcast(F32)).then_inc(b_done[r], 16)

            def store_y(b, more=0):
                sp.wait_ge(mlp_act, ordinal(b, BATCHES - 2) + 1 + more)
                sp.dma_start(out[:, bass.ts(b - 1, PB)], y[:, :]).then_inc(y_out, 16)

            load_idx(0, 0)
            for c in range(KRING):
                load_k(c)
            load_idx(1, 1)
            for c in range(KRING, K_LEAD):
                load_k(c)
            swap_halves(0, 0)

            def body(b, first, last):
                for u in range(2):
                    t = 2 * b + u
                    for s in range(NS):
                        if first and u == 0:
                            for c in k_before(s, K_LEAD + KRING):
                                if c >= K_LEAD:
                                    load_k(c)
                            if s == 0:
                                swap_halves(1, 1)
                            if s == 2:
                                load_dense(0, 0)
                                load_dense(1, 1)
                            if s == 13:
                                sp.wait_ge(k_done, K_GPSIMD)
                                sp.wait_ge(k_done_pool, NS - K_GPSIMD)
                                sp.dma_start(w1[:, :, :], W1.rearrange("(k p) m -> p k m", p=P)).then_inc(weights_in, 16)
                                sp.dma_start(w2[:, :, :], W2.rearrange("(k p) m -> p k m", p=P)).then_inc(weights_in, 16)
                                sp.dma_start(w3[:, :], W3).then_inc(weights_in, 16)
                                sp.dma_start(b1c[:, :], b1).then_inc(weights_in, 16)
                                sp.dma_start(b2c[:, :], b2).then_inc(weights_in, 16)
                        if s == (12, 30)[u] and not (first and u == 0) and not (last and u == 1):
                            sp.wait_ge(mlp_pe, z_read(b - 1 + u, 1 - u))
                            load_dense(t + 1, 1 - u)
                        if s == 26 and not last:
                            sp.wait_ge(mult_done, NS * t + max(GATHERS_AT) + 1)
                            load_idx(t + 2, u)
                        if s in TR_AT:
                            ahead, q = TR_AT[s]
                            if not (last and u == 1 and ahead):
                                swap_halves(QUADS * (t + ahead) + q, q % ERING)
                        if u == 1 and s == 26 and not first:
                            store_y(b)

            bodies(sp, body)
            store_y(BODIES, 1)
            sp.wait_ge(y_out, 16 * BODIES)

        @block.gpsimd
        def _(pool):
            def gather(u, start, end):
                for f in range(start, end):
                    nc.gpsimd.indirect_dma_start(
                        out=E[:, u, f, :], out_offset=None, in_=tables[f],
                        in_offset=bass.IndirectOffsetOnAxis(ap=idx[:, u, f:f + 1].bitcast(U32), axis=0),
                    ).then_inc(gathered[u][f // QF], 16)

            def low(Q, u, q):
                pool.wait_ge(cast_done, Q + 1)
                nc.gpsimd.tensor_tensor(nat[:, q % 2, :, 1, :], E[:, u, QF * q:QF * q + QF, :],
                                        nat[:, q % 2, :, 0, :].bitcast(F32), ALU.subtract).then_inc(low_done, 1)

            nc.gpsimd.memset(ident_start, 0.0).then_inc(ident_0, 1)
            pool.wait_ge(idx_in[0], 16)
            gather(0, 0, QF)
            pool.wait_ge(ident_0, 1)
            nc.gpsimd.affine_select(out=ident_start, in_=ident_start, compare_op=ALU.not_equal, fill=1.0,
                                    base=0, pattern=[[-1, P]], channel_multiplier=1).then_inc(ident_1, 1)
            for q in range(1, QUADS):
                gather(0, QF * q, QF * q + QF)
                if q in LOW_AFTER:
                    Q = LOW_AFTER.index(q)
                    low(Q, 0, Q)

            def halve(t, u, s):
                pool.wait_ge(mult_done, NS * t + s + 1)
                x = prod[:, place(u, s), :].rearrange("p (n h) -> p n h", h=D)
                nc.gpsimd.tensor_tensor(x[:, :, 0:D // 2], x[:, :, 0:D // 2], x[:, :, D // 2:D], ALU.add).then_inc(halved, 1)

            def low_k(quads):
                pool.wait_ge(low_done, quads)
                for c in range(K_GPSIMD, NS):
                    pool.wait_ge(kh_done, c + 1)
                    nc.gpsimd.tensor_tensor(kst[D:P, k_cols(c)], raw[c % KRING][:, 0:len(SLOTS[c][1]) * D],
                                            kst[0:D, k_cols(c)].bitcast(F32), ALU.subtract).then_inc(k_done_pool, 1)
                pool.wait_ge(k_done_pool, NS - K_GPSIMD)

            ORDER = [(k + 1, "halve", k) for k in HALVED] + [(0, "low", (0, 3))]
            ORDER += [(at + 1, "low", which) for at, which in CAST_AT.items() if at + 1 < 28]
            ORDER += [(GATHER_FROM + GATHER_STEP * f, "gather", f) for f in range(NF)]
            ORDER.append((K_GPSIMD_AT, "k", None))
            ORDER.sort(key=lambda x: x[0])

            def body(b, first, last):
                for u in range(2):
                    t = 2 * b + u
                    more = not (last and u == 1)
                    if not (first and u == 0):
                        low(QUADS * t + 2, u, 2)
                    if more:
                        pool.wait_ge(idx_in[1 - u], 16 * (b + 1 + u))
                        if not (first and u == 0):
                            pool.wait_ge(mult_done, NS * t)
                    for _, what, x in ORDER:
                        if what == "low" and (more or not x[0]) and not (first and u == 0 and x == (0, 3)):
                            low(QUADS * (t + x[0]) + x[1], u ^ x[0], x[1])
                        if what == "k" and first and u == 0:
                            low_k(4 + sum(at + 1 < K_GPSIMD_AT for at, x in CAST_AT.items() if x[1] >= 4 and not x[0]))
                        if what == "gather" and more:
                            gather(1 - u, x, x + 1)
                        if what == "halve" and not (first and u == 0):
                            halve(t, u, x)

            bodies(pool, body)

        @block.scalar
        def _(act):
            def cast_k(cs):
                for c in cs:
                    act.wait_ge(k_in[c % KRING], 16 * (c // KRING + 1))
                    nc.scalar.activation(kst[0:D, k_cols(c)], raw[c % KRING][:, 0:len(SLOTS[c][1]) * D],
                                         ACT.Copy).then_inc(kh_done, 1)

            def cast(Q, b, u, q, start=False):
                act.wait_ge(gathered[u][q], 16 * QF * (b + 1))
                if not start:
                    act.wait_ge(e_transposed, Q - 1)
                nc.scalar.activation(nat[:, q % 2, :, 0, :], E[:, u, QF * q:QF * q + QF, :],
                                     ACT.Copy).then_inc(cast_done, 1)

            def evacuate_quad(Q, q):
                act.wait_ge(e_transposed, Q + 1)
                fields = min(QF, NF - 1 - QF * q)
                nc.scalar.activation(eA[:, q % ERING, 0:fields, :],
                                     psE[:, 0:fields * P].rearrange("p (f b) -> p f b", b=P),
                                     ACT.Copy).then_inc(a_done, 1)

            def mlp_evacuate(b, batch):
                act.wait_ge(mlp_pe, ordinal(b, batch) + 1)
                what, m = MLP[batch]
                if what == "z":
                    last = nc.scalar.activation(zT[:, :, m * P:(m + 1) * P], psM[:, :].rearrange("p (k b) -> p k b", k=KC), ACT.Copy)
                elif what == "layer1":
                    last = nc.scalar.activation(h1T[:, m, :], psM[:, 0:PB], ACT.Relu, bias=b1c[:, m:m + 1])
                elif what == "layer2":
                    last = nc.scalar.activation(h2T[:, m, :], psM[:, 0:PB], ACT.Relu, bias=b2c[:, m:m + 1])
                else:
                    last = nc.scalar.activation(y[:, :], psM[0:1, 0:PB], ACT.Copy)
                last.then_inc(mlp_act, 1)

            def reduce(t, u, s):
                n, size = SLOTS[s][0], len(SLOTS[s][1])
                act.wait_ge(mult_done, NS * t + s + 1)
                for m in range(share(size), size):
                    x = prod[:, place(u, s), m * D:(m + 1) * D]
                    last = nc.scalar.activation(x, x, ACT.Copy, accum_out=z[:, u, n + m:n + m + 1])
                last.then_inc(act_reduced, 1)

            cast_k(range(0, 5))
            cast(0, 0, 0, 0, start=True)
            cast_k(range(5, 8))
            evacuate_quad(0, 0)
            cast_k(range(8, 9))
            cast(1, 0, 0, 1, start=True)

            def body(b, first, last):
                for u in range(2):
                    t = 2 * b + u
                    more = not (last and u == 1)
                    for s in range(NS):
                        if first and u == 0:
                            cast_k(c for c in k_before(s, K_LEAD + K_AHEAD) if c >= 9)
                            if s == 0:
                                evacuate_quad(1, 1)
                            if s in START_CAST_AT:
                                cast(START_CAST_AT[s], 0, 0, START_CAST_AT[s])
                        if s in QUAD_EVAC_AT:
                            ahead, q = QUAD_EVAC_AT[s]
                            if more or not ahead:
                                evacuate_quad(QUADS * (t + ahead) + q, q)
                        if s in CAST_AT:
                            ahead, q = CAST_AT[s]
                            if more or not ahead:
                                bb, uu = (b, u) if not ahead else (b, 1) if u == 0 else (b + 1, 0)
                                cast(QUADS * (t + ahead) + q, bb, uu, q)
                        batch = MLP_EVAC_AT.get((u, s))
                        if first and batch == BATCHES - 1:
                            act.wait_ge(weights_in, 5 * 16)
                        if batch is not None and (batch == BATCHES - 1 or not first):
                            mlp_evacuate(b, batch)
                        if u == 1 and s == 31 and not first:
                            act.wait_ge(y_out, 16 * b)
                        if s == 0 and not (first):
                            act.wait_ge(mlp_pe, z_read(b - 1, u))
                        if s in SHARED:
                            reduce(t, u, s)

            bodies(act, body)
            act.wait_ge(mlp_pe, END + 2)
            nc.scalar.activation(zT[:, :, P:PB], free_bank(0).rearrange("p (k b) -> p k b", k=KC), ACT.Copy).then_inc(mlp_act, 1)
            for m in range(M1):
                last = nc.scalar.activation(h1T[:, m, 0:P], psM[:, m * P:(m + 1) * P], ACT.Relu, bias=b1c[:, m:m + 1])
            last.then_inc(mlp_act, 1)
            for m in range(M1):
                act.wait_ge(mlp_pe, END + 3 + m)
                nc.scalar.activation(h1T[:, m, P:PB], free_bank(1 + m)[:, 0:P], ACT.Relu, bias=b1c[:, m:m + 1]).then_inc(mlp_act, 1)
            for m in range(M2):
                act.wait_ge(mlp_pe, END + 3 + M1 + m)
                nc.scalar.activation(h2T[:, m, :], free_bank((5 + m) % 6)[:, 0:PB], ACT.Relu, bias=b2c[:, m:m + 1]).then_inc(mlp_act, 1)
            act.wait_ge(mlp_pe, END + 3 + M1 + M2)
            nc.scalar.activation(y[:, :], free_bank(1)[0:1, 0:PB], ACT.Copy).then_inc(mlp_act, 1)

        @block.vector
        def _(dve):
            def low_k(c):
                dve.wait_ge(kh_done, c + 1)
                nc.vector.tensor_tensor(kst[D:P, k_cols(c)], raw[c % KRING][:, 0:len(SLOTS[c][1]) * D],
                                        kst[0:D, k_cols(c)].bitcast(F32), ALU.subtract).then_inc(k_done, 1)

            def multiply(b, t, u, s, first):
                _, pairs, i, j = SLOTS[s]
                for q in GATHERS_AT.get(s, []):
                    dve.wait_ge(gathered[u][q], 16 * QF * (b + 1))
                dve.wait_ge(t_ready, NS * t + s + 1)
                early = first and u == 0
                if s in SUMMED:
                    k = SUMMED.index(s)
                    if not (early and k < SUMMED_RING):
                        dve.wait_ge(summed, len(SUMMED) * t + k - SUMMED_RING + 1)
                else:
                    k = SHARED.index(s)
                    if not (early and k < SHARED_RING):
                        before = len(SHARED) * t + k - SHARED_RING + 1
                        dve.wait_ge(act_reduced, before)
                        dve.wait_ge(dve_reduced, before)
                p, t_slot = prod[:, place(u, s), :], T[:, s % T_RING, :]
                if j is not None:
                    last = nc.vector.tensor_tensor(
                        p.rearrange("p (i x) -> p i x", i=QF), t_slot.rearrange("p (i x) -> p i x", i=QF),
                        E[:, u, QF * j:QF * j + QF, :].rearrange("p f h -> p (f h)").unsqueeze(1).broadcast_to([P, QF, QF * D]),
                        ALU.mult)
                else:
                    two = E[:, u, QF * i:QF * i + 2 * QF, :]
                    x = 0
                    if len(pairs) >= SLOT // 2:
                        x = 8 * D
                        last = nc.vector.tensor_tensor(
                            p[:, 0:x].rearrange("p (q i x) -> p q i x", q=2, i=2), t_slot[:, 0:x].rearrange("p (q i x) -> p q i x", q=2, i=2),
                            two.rearrange("p (q f) h -> p q (f h)", q=2)[:, :, 2 * D:4 * D].unsqueeze(2).broadcast_to([P, 2, 2, 2 * D]),
                            ALU.mult)
                    if len(pairs) != SLOT // 2:
                        y = x + QF * D
                        last = nc.vector.tensor_tensor(
                            p[:, x:y].rearrange("p (k h) -> p k h", k=QF), t_slot[:, x:y].rearrange("p (k h) -> p k h", k=QF),
                            two.rearrange("p (k a) h -> p k a h", a=2)[:, :, 1, :], ALU.mult)
                last.then_inc(mult_done, 1)

            def reduce(t, u, s):
                n, size = SLOTS[s][0], len(SLOTS[s][1])
                k = share(size)
                dve.wait_ge(mult_done, NS * t + s + 1)
                nc.vector.tensor_reduce(z[:, u, n:n + k], prod[:, place(u, s), 0:k * D].rearrange("p (n h) -> p n h", h=D),
                                        AX_X, ALU.add).then_inc(dve_reduced, 1)

            def fold(t, u, s):
                n, size = SLOTS[s][0], len(SLOTS[s][1])
                k = SUMMED.index(s)
                dve.wait_ge(summed, len(SUMMED) * t + k + 1)
                nc.vector.tensor_reduce(z[:, u, n:n + size], psZ[:, :, :],
                                        AX_X, ALU.add).then_inc(folded, 1)

            def after_slot(t, u, s, first, past=False):
                for back, k in FOLD_AT.get(s, []):
                    if not (first and back) and not (past and not back):
                        fold(t - back, u ^ back, k)
                for back, k in REDUCE_AT.get(s, []):
                    if not (first and back) and not (past and not back):
                        reduce(t - back, u ^ back, k)

            for c in range(3):
                low_k(c)
            dve.wait_ge(ident_1, 1)
            nc.vector.tensor_copy(identr[:, :], ident_start).then_inc(identr_done, 1)

            def body(b, first, last):
                for u in range(2):
                    t = 2 * b + u
                    for s in range(NS):
                        if first and u == 0:
                            for c in k_before(s, K_LEAD):
                                if 3 <= c < K_GPSIMD:
                                    low_k(c)
                        multiply(b, t, u, s, first)
                        if s == 1 and not first:
                            dve.wait_ge(mlp_pe, z_read(b - 1, u))
                        after_slot(t, u, s, first and u == 0)

            bodies(dve, body)
            for s in range(PAST):
                after_slot(TILES, 0, s, False, past=True)

        @block.tensor
        def _(pe):
            def transpose_quad(Q, q, batches=None):
                pe.wait_ge(low_done, Q + 1)
                if not (isinstance(Q, int) and Q == 0):
                    pe.wait_ge(a_done, Q)
                if batches is not None:
                    pe.wait_ge(mlp_act, batches)
                for f in range(min(QF, NF - 1 - QF * q)):
                    last = nc.tensor.transpose(psE[:, f * P:(f + 1) * P].bitcast(F32R),
                                               nat[:, q % 2, f, :, :].rearrange("p a h -> p (a h)"), identr[:, :])
                last.then_inc(e_transposed, 1)

            def products(t, s, first):
                n, pairs = SLOTS[s][0], SLOTS[s][1]
                if first:
                    if s < K_GPSIMD:
                        pe.wait_ge(k_done, s + 1)
                    else:
                        pe.wait_ge(k_done_pool, s - K_GPSIMD + 1)
                for q in range(QUADS):
                    if first_use[q] == s:
                        pe.wait_ge(b_done[q % ERING], 32 * (QUADS // ERING * t + q // ERING + 1))
                if not (first and s < T_RING):
                    pe.wait_ge(mult_done, NS * t + s - T_RING + 1)
                for i, m, w in runs(pairs):
                    o = T[:, s % T_RING, m * D:(m + w) * D]
                    rhs = kst[:, (n + m) * D:(n + m + w) * D]
                    nc.tensor.matmul(o, eA[:, i // QF % ERING, i % QF, :], rhs, start=True, stop=False)
                    last = nc.tensor.matmul(o, eB[:, i // QF % ERING, i % QF, :], rhs, start=False, stop=True)
                last.then_inc(t_ready, 1)

            def sum_products(t, u, s):
                j = SUMMED.index(s)
                steps = D // FOLD
                if s in HALVED and not (isinstance(t, int) and t == 0):
                    steps //= 2
                    pe.wait_ge(halved, len(HALVED) * (t - 1) + HALVED.index(s) + 1)
                else:
                    pe.wait_ge(mult_done, NS * t + s + 1)
                if not (isinstance(t, int) and t == 0 and j == 0):
                    pe.wait_ge(folded, len(SUMMED) * t + j)
                for k in range(steps):
                    x = prod[:, place(u, s), :].rearrange("p (n h) -> p n h", h=D)[:, :, k * FOLD:(k + 1) * FOLD]
                    last = nc.tensor.matmul(psZ[:, :, :], ident, x, start=(k == 0), stop=(k == steps - 1))
                last.then_inc(summed, 1)

            def transpose_z(t, u, b, bank):
                pe.wait_ge(dve_reduced, len(SHARED) * (t + 1))
                pe.wait_ge(act_reduced, len(SHARED) * (t + 1))
                pe.wait_ge(folded, len(SUMMED) * (t + 1))
                pe.wait_ge(dense_in[u], 16 * (b + 1 if u == 0 else b))
                for k in range(KC):
                    last = nc.tensor.transpose(bank[:, k * P:(k + 1) * P], z[:, u, k * P:(k + 1) * P], ident)
                last.then_inc(mlp_pe, 1)

            def layer(o, w, src, blocks, ready=None):
                for k in range(blocks):
                    if ready is not None:
                        pe.wait_ge(mlp_act, ready + k)
                    last = nc.tensor.matmul(o, w(k), src[:, k, :], start=(k == 0), stop=(k == blocks - 1))
                last.then_inc(mlp_pe, 1)

            def mlp_batch(b, batch, quads):
                what, m = MLP[batch]
                pe.wait_ge(a_done, quads)
                if not (isinstance(b, int) and b == 0):
                    pe.wait_ge(mlp_act, ordinal(b, batch))
                if what == "z":
                    transpose_z(2 * b - m, m, b, psM)
                elif what == "layer1":
                    layer(psM[:, 0:PB], lambda k: w1[:, k, m * P:(m + 1) * P], zT, KC)
                elif what == "layer2":
                    layer(psM[:, 0:PB], lambda k: w2[:, k, m * P:(m + 1) * P], h1T, M1)
                else:
                    layer(psM[0:1, 0:PB], lambda k: w3[:, k:k + 1], h2T, M2)

            pe.wait_ge(identr_done, 1)
            transpose_quad(0, 0)
            transpose_quad(1, 1)

            def body(b, first, last):
                for u in range(2):
                    t = 2 * b + u
                    more = not (last and u == 1)
                    for s in range(NS):
                        products(t, s, first and u == 0)
                        if s in TR_AT:
                            ahead, q = TR_AT[s]
                            if more or not ahead:
                                batches = batches_before(u, s)
                                if first and batches < BATCHES:
                                    batches = None
                                else:
                                    batches = ordinal(b, batches)
                                transpose_quad(QUADS * (t + ahead) + q, q, batches)
                        for back, k in SUM_AT.get(s, []):
                            if not (first and u == 0 and back):
                                sum_products(t - back, u ^ back, k)
                        if (u, s) in MLP_AT:
                            batch = MLP_AT[u, s]
                            if first and batch == BATCHES - 1:
                                pe.wait_ge(weights_in, 5 * 16)
                            if batch == BATCHES - 1 or not first:
                                mlp_batch(b, batch, QUADS * t + 2 + quads_before(s))

            bodies(pe, body)

            def layer1_even(m):
                for k in range(KC):
                    last = nc.tensor.matmul(psM[:, m * P:(m + 1) * P], w1[:, k, m * P:(m + 1) * P], zT[:, k, 0:P],
                                            start=(k == 0), stop=(k == KC - 1))
                return last

            pe.wait_ge(mlp_act, END)
            for m in range(M1 // 2):
                layer1_even(m)
            for s in range(PAST):
                for back, k in SUM_AT.get(s, []):
                    if back:
                        sum_products(TILES - back, 1, k)
            for m in range(M1 // 2, M1):
                last = layer1_even(m)
            last.then_inc(mlp_pe, 1)
            transpose_z(TILES - 1, 1, BODIES, free_bank(0))
            pe.wait_ge(mlp_act, END + 1)
            for m in range(M1):
                layer(free_bank(1 + m)[:, 0:P], lambda k: w1[:, k, m * P:(m + 1) * P], zT[:, :, P:PB], KC)
            for m in range(M2):
                layer(free_bank((5 + m) % 6)[:, 0:PB], lambda k: w2[:, k, m * P:(m + 1) * P], h1T, M1, END + 3)
            layer(free_bank(1)[0:1, 0:PB], lambda k: w3[:, k:k + 1], h2T, M2, END + 3 + M1)


def kernel(**inputs):
    import numpy as np
    import concourse.bacc as bacc
    from concourse.bass_utils import run_bass_kernel_spmd

    nc = bacc.Bacc("TRN2", target_bir_lowering=False, num_devices=1)
    arrays = {}

    def given(name, a):
        a = np.ascontiguousarray(a)
        arrays[name] = a
        return nc.dram_tensor(name, a.shape, mybir.dt.from_np(a.dtype), kind="ExternalInput").ap()

    fields = inputs["ids"].shape[1]
    args = [given(n, inputs[n]) for n in ("dense_ctx", "ids")]
    args.append([given(f"tbl_{f}", inputs[f"tbl_{f}"]) for f in range(fields)])
    order = [i * (fields - 1) - i * (i - 1) // 2 + j - i - 1 for _, pairs, _, _ in plan(fields) for i, j in pairs]
    W1 = np.asarray(inputs["W_top1"])
    args += [given("W_top1", np.concatenate([W1[order], W1[len(order):]])), given("b_top1", np.asarray(inputs["b_top1"]).reshape(-1, P).T),
             given("W_top2", inputs["W_top2"]), given("b_top2", np.asarray(inputs["b_top2"]).reshape(-1, P).T),
             given("W_top3", np.asarray(inputs["W_top3"]).reshape(-1, P).T)]
    k = np.asarray(inputs["L0_rec_kernel"])
    args.append(given("K_T", k.transpose(2, 1, 0)[:, order].reshape(k.shape[2], -1)))
    batch = inputs["ids"].shape[0]
    out = nc.dram_tensor("y_out_dram", (1, batch), F32, kind="ExternalOutput").ap()
    dlrm_tower(nc, *args, out)
    r = run_bass_kernel_spmd(nc, [arrays], core_ids=[0])
    return r.results[0]["y_out_dram"].reshape(batch, 1)
```
